# Optimizing a Trainium2 kernel written in Bass

```python
import numpy as np
import jax
import jax.numpy as jnp

def _softmax(x, axis=-1):
    return jax.nn.softmax(x, axis=axis)

def _gelu(x):
    return jax.nn.gelu(x, approximate=True)

def _silu(x):
    return jax.nn.silu(x)

def _sigmoid(x):
    return jax.nn.sigmoid(x)

def _layernorm(x, axis=-1, eps=1e-05):
    m = jnp.mean(x, axis=axis, keepdims=True)
    v = jnp.var(x, axis=axis, keepdims=True)
    return (x - m) / jnp.sqrt(v + eps)

def _scatter_add(tgt, idx, src, axis=0):
    return tgt.at[idx].add(src)

def _segment_sum(src, seg, n):
    return jax.ops.segment_sum(src, seg, n)
kernel_name = 'mk_cond_resid_d1_seqx_r4_1c1c8f'

def setup_inputs(seed: int=0):
    np.random.seed(seed)
    _w = jnp.asarray

    def _rec_inputs():
        import jax
        import jax.numpy as jnp
        _rk = jax.random.key(seed)
        x = 4.136e-05 + 0.9999 * jax.random.normal(jax.random.fold_in(_rk, 1), (128, 64, 256), jnp.float32)
        _lenS = 64 - jax.random.randint(jax.random.fold_in(_rk, 7), (128,), 0, max(1, 64 // 4) + 1, jnp.int32)
        _lenS2 = 64 - jax.random.randint(jax.random.fold_in(_rk, 8), (128,), 0, max(1, 64 // 4) + 1, jnp.int32)
        cond_1024 = -0.00608245 + 1.00131 * jax.random.normal(jax.random.fold_in(_rk, 11), (128, 256), jnp.float32)
        return (x, cond_1024)
    x, cond_1024 = _rec_inputs()

    def _L0_cond_setup():
        import jax, jax.numpy as jnp
        import numpy as np
        B, T, D_IN, V_IN, E = (64, 128, 256, 256, 256)
        key = jax.random.key(seed)
        ks = jax.random.split(key, 16)
        s = 0.01
        return {'video': jax.random.normal(ks[0], (B, V_IN), jnp.float32), 'seq': jax.random.normal(ks[1], (B, T, D_IN), jnp.float32), 'W_z': jax.random.normal(ks[2], (D_IN, E), jnp.float32) * s, 'U_z': jax.random.normal(ks[3], (E, E), jnp.float32) * s, 'C_z': jax.random.normal(ks[4], (V_IN, E), jnp.float32) * s, 'b_z': jnp.zeros((E,), jnp.float32), 'W_r': jax.random.normal(ks[5], (D_IN, E), jnp.float32) * s, 'U_r': jax.random.normal(ks[6], (E, E), jnp.float32) * s, 'C_r': jax.random.normal(ks[7], (V_IN, E), jnp.float32) * s, 'b_r': jnp.zeros((E,), jnp.float32), 'W': jax.random.normal(ks[8], (D_IN, E), jnp.float32) * s, 'U': jax.random.normal(ks[9], (E, E), jnp.float32) * s, 'C': jax.random.normal(ks[10], (V_IN, E), jnp.float32) * s, 'b': jnp.zeros((E,), jnp.float32)}
    _L0_cond_all = _L0_cond_setup()
    _L0_cond_in = {k: v for k, v in _L0_cond_all.items() if k in ('W_z', 'U_z', 'C_z', 'b_z', 'W_r', 'U_r', 'C_r', 'b_r', 'W', 'U', 'C', 'b')}
    del _L0_cond_all
    return {'x': x, 'cond_1024': cond_1024, 'L0_cond_W_z': _L0_cond_in['W_z'], 'L0_cond_U_z': _L0_cond_in['U_z'], 'L0_cond_C_z': _L0_cond_in['C_z'], 'L0_cond_b_z': _L0_cond_in['b_z'], 'L0_cond_W_r': _L0_cond_in['W_r'], 'L0_cond_U_r': _L0_cond_in['U_r'], 'L0_cond_C_r': _L0_cond_in['C_r'], 'L0_cond_b_r': _L0_cond_in['b_r'], 'L0_cond_W': _L0_cond_in['W'], 'L0_cond_U': _L0_cond_in['U'], 'L0_cond_C': _L0_cond_in['C'], 'L0_cond_b': _L0_cond_in['b']}

def reference(x, cond_1024, L0_cond_W_z, L0_cond_U_z, L0_cond_C_z, L0_cond_b_z, L0_cond_W_r, L0_cond_U_r, L0_cond_C_r, L0_cond_b_r, L0_cond_W, L0_cond_U, L0_cond_C, L0_cond_b):
    import jax
    import jax.numpy as jnp

    def _L0_cond_ref(video, seq, W_z, U_z, C_z, b_z, W_r, U_r, C_r, b_r, W, U, C, b):
        import jax, jax.numpy as jnp
        import numpy as np
        B, T, D_IN, V_IN, E = (64, 128, 256, 256, 256)
        vz = video @ C_z + b_z
        vr = video @ C_r + b_r
        vh = video @ C + b
        xz = jnp.einsum('btd,de->bte', seq, W_z)
        xr = jnp.einsum('btd,de->bte', seq, W_r)
        xh = jnp.einsum('btd,de->bte', seq, W)

        def step(h, xs):
            xzt, xrt, xht = xs
            z = jax.nn.sigmoid(xzt + h @ U_z + vz)
            r = jax.nn.sigmoid(xrt + h @ U_r + vr)
            hh = jnp.tanh(xht + r * h @ U + vh)
            h_new = (1.0 - z) * h + z * hh
            return (h_new, h_new)
        h0 = jnp.zeros((seq.shape[0], U.shape[0]), seq.dtype)
        xs = (jnp.swapaxes(xz, 0, 1), jnp.swapaxes(xr, 0, 1), jnp.swapaxes(xh, 0, 1))
        _, out_t = jax.lax.scan(step, h0, xs)
        return jnp.swapaxes(out_t, 0, 1)
    x = x + _L0_cond_ref(cond_1024, x, L0_cond_W_z, L0_cond_U_z, L0_cond_C_z, L0_cond_b_z, L0_cond_W_r, L0_cond_U_r, L0_cond_C_r, L0_cond_b_r, L0_cond_W, L0_cond_U, L0_cond_C, L0_cond_b)
    return x

_drawn_inputs = setup_inputs


def setup_inputs(seed=0):
    import zlib

    import numpy as np

    out = dict(_drawn_inputs(seed))
    spreads = {'L0_cond_b_z': (0.0, 0.8), 'L0_cond_b_r': (0.0, 2.0), 'L0_cond_b': (0.0, 0.1)}
    factors = {'L0_cond_W_z': 7.153,
     'L0_cond_U_z': 45.033,
     'L0_cond_C_z': 8.0,
     'L0_cond_W_r': 25.469,
     'L0_cond_U_r': 64.0,
     'L0_cond_C_r': 8.0,
     'L0_cond_U': 4.04}
    for name, (base, spread) in spreads.items():
        noise = np.random.default_rng([zlib.crc32(name.encode()), seed]).standard_normal(out[name].shape)
        drawn = base * np.exp(spread * noise) if base else spread * noise
        out[name] = jnp.asarray(drawn.astype(out[name].dtype))
    for name, factor in factors.items():
        out[name] = (out[name] * factor).astype(out[name].dtype)
    return out
```

```python
from contextlib import ExitStack

import concourse.bass as bass
from concourse import mybir

ALU = mybir.AluOpType
ACT = mybir.ActivationFunctionType
F32 = mybir.dt.float32
F32R = mybir.dt.float32r

P = 128
NC = 2
PAIR = 2
RING = 4
R, H, Z = 0, 1, 2
TILES = [(R, 0), (H, 0), (R, 1), (H, 1), (Z, 0), (Z, 1)]


def gated_recurrence(nc, x, cond, Wz, Uz, Cz, bz, Wr, Ur, Cr, br, W, U, C, b, out):
    B, T, D = x.shape
    E = U.shape[1]
    PAIRS = T // PAIR
    TURNS = PAIRS // RING
    assert B == P and D == NC * P and E == NC * P and TURNS * RING * PAIR == T
    Ws, Us, Cs, bs = (Wr, W, Wz), (Ur, U, Uz), (Cr, C, Cz), (br, b, bz)

    with ExitStack() as ctx:
        def sb(name, shape, dt=F32):
            return ctx.enter_context(nc.sbuf_tensor(name, shape, dt))

        def pb(name, shape):
            return ctx.enter_context(nc.psum_tensor(name, shape, F32))

        def sem(name):
            return ctx.enter_context(nc.semaphore(name))

        w_raw = sb("w_raw", [P, 3, NC, E])
        w_hi = sb("w_hi", [P, 3, NC, E], F32R)
        w_lo = sb("w_lo", [P, 3, NC, E], F32R)
        u = sb("u", [P, 3, NC, E])
        c_w = sb("c_w", [P, 3, NC, E])
        bias = sb("bias", [P, 3, NC])
        cond_sb = sb("cond_sb", [B, NC * P])
        cond_t = sb("cond_t", [P, NC, B])
        ident = sb("ident", [P, P])
        v = sb("v", [P, len(TILES), PAIR, B])
        x_ring = sb("x_ring", [B, RING, PAIR, D])
        y_ring = sb("y_ring", [B, RING, PAIR, E])
        xt_hi = sb("xt_hi", [P, 2, NC, PAIR * B], F32R)
        xt_lo = sb("xt_lo", [P, 2, NC, PAIR * B], F32R)
        h = sb("h", [P, 2, NC, B])
        r = sb("r", [P, NC, B])
        z = sb("z", [P, NC, B])
        rh = sb("rh", [P, NC, B])
        hh = sb("hh", [P, NC, B])
        zhh = sb("zhh", [P, NC, B])
        zh = sb("zh", [P, NC, B])

        pre = [[pb(f"pre{s}{k}", [P, 2, PAIR, B]) for k in range(3)] for s in range(2)]
        x_ps = pb("x_ps", [P, NC, PAIR * B])
        y_ps = pb("y_ps", [P, 2, E])

        def tile_of(s, i):
            return pre[s][i // 2][:, i % 2]

        def pre_of(s, gate, m):
            return tile_of(s, TILES.index((gate, m)))

        u_loaded = sem("u_loaded")
        w_loaded = sem("w_loaded")
        cond_loaded = sem("cond_loaded")
        x_loaded = [sem(f"x_loaded{k}") for k in range(RING)]
        y_stored = [sem(f"y_stored{k}") for k in range(RING)]
        zeroed = sem("zeroed")
        ident_ready = sem("ident_ready")
        h0_ready = sem("h0_ready")
        w_hi_ready = sem("w_hi_ready")
        w_lo_ready = sem("w_lo_ready")
        banks_marked = sem("banks_marked")
        cond_turned = sem("cond_turned")
        cond_t_ready = sem("cond_t_ready")
        v_summed = sem("v_summed")
        v_ready = sem("v_ready")
        seeded = sem("seeded")
        x_turned = sem("x_turned")
        xt_hi_ready = sem("xt_hi_ready")
        xt_lo_ready = sem("xt_lo_ready")
        r_summed = sem("r_summed")
        z_summed = sem("z_summed")
        hh_summed = sem("hh_summed")
        r_ready = sem("r_ready")
        z_ready = sem("z_ready")
        hh_ready = sem("hh_ready")
        rh_ready = sem("rh_ready")
        zh_ready = sem("zh_ready")
        zhh_ready = sem("zhh_ready")
        h_ready = sem("h_ready")
        h_turned = sem("h_turned")
        y_ready = sem("y_ready")

        def turns(eng, body):
            with eng.Fori(0, TURNS - 1) as i:
                body(i * RING, i, False)
            body((TURNS - 1) * RING, TURNS - 1, True)

        block = ctx.enter_context(nc.Block())

        @block.sync
        def _(sp):
            def load_pair(pair, slot):
                sp.dma_start(x_ring[:, slot], x[:, bass.ds(pair * PAIR, PAIR), :]).then_inc(x_loaded[slot], 16)

            for k in range(RING):
                sp.sem_inc(y_stored[k], 16)
            sp.dma_start(cond_sb[:], cond).then_inc(cond_loaded, 16)
            sp.dma_start(x_ring[:, 0], x[:, 0:PAIR, :]).then_inc(x_loaded[0], 16)
            for g in range(3):
                sp.dma_start(w_raw[:, g], Ws[g].rearrange("(k p) e -> p k e", p=P)).then_inc(w_loaded, 16)
            for k in range(1, RING):
                load_pair(k, k)
            for g in range(3):
                sp.dma_start(u[:, g], Us[g].rearrange("(k p) e -> p k e", p=P)).then_inc(u_loaded, 16)

            def body(pair0, turn, last):
                for k in range(RING):
                    sp.wait_ge(y_ready, PAIR * (pair0 + k + 1) + 2)
                    sp.dma_start(out[:, bass.ds((pair0 + k) * PAIR, PAIR), :], y_ring[:, k]).then_inc(y_stored[k], 16)
                    if not last:
                        load_pair(pair0 + k + RING, k)

            turns(sp, body)
            for k in range(RING):
                sp.wait_ge(y_stored[k], 16 * (TURNS + 1))

        @block.gpsimd
        def _(pool):
            nc.gpsimd.memset(ident[:], 0.0).then_inc(zeroed, 1)
            pool.wait_ge(zeroed, 1)
            nc.gpsimd.affine_select(out=ident[:], in_=ident[:], compare_op=ALU.not_equal, fill=1.0, base=0,
                                    pattern=[[-1, P]], channel_multiplier=1).then_inc(ident_ready, 1)

        @block.tensor
        def _(pe):
            def turn_x(pair, s, slot, turn):
                pe.wait_ge(x_loaded[slot], 16 * (turn + 1))
                if not (isinstance(pair, int) and pair == 0):
                    pe.wait_ge(xt_lo_ready, NC * pair)
                for c in range(NC):
                    for j in range(PAIR):
                        mm = nc.tensor.transpose(x_ps[:, c, j * B:(j + 1) * B],
                                                 x_ring[:, slot, j, c * P:(c + 1) * P], ident[:])
                mm.then_inc(x_turned, 1)

            def project(pair, s, tiles):
                for i in tiles:
                    g, m = TILES[i]
                    cols = slice(m * P, (m + 1) * P)
                    pe.wait_ge(seeded, len(TILES) * pair + 2 * (i // 2) + 2)
                    if i == 0:
                        pe.wait_ge(xt_hi_ready, pair + 1)
                    dst = tile_of(s, i)
                    for k in range(NC):
                        nc.tensor.matmul(dst, w_hi[:, g, k, cols], xt_hi[:, s, k], start=False, stop=False,
                                         skip_group_check=True)
                        nc.tensor.matmul(dst, w_lo[:, g, k, cols], xt_hi[:, s, k], start=False, stop=False,
                                         skip_group_check=True)
                    if i == 0:
                        pe.wait_ge(xt_lo_ready, NC * (pair + 1))
                    for k in range(NC):
                        nc.tensor.matmul(dst, w_hi[:, g, k, cols], xt_lo[:, s, k], start=False, stop=False,
                                         skip_group_check=True)

            def times_u(g, s, j, moving, k, m):
                return nc.tensor.matmul(pre_of(s, g, m)[:, j], u[:, g, k, m * P:(m + 1) * P], moving,
                                        start=False, stop=(k == NC - 1), skip_group_check=True)

            def turn_h(t, par):
                pe.wait_ge(y_ready, t + 1)
                pe.wait_ge(h_ready, NC * (t + 1))
                for c in range(NC):
                    mm = nc.tensor.transpose(y_ps[:, par, c * P:(c + 1) * P], h[:, par, c], ident[:])
                mm.then_inc(h_turned, 1)

            pe.wait_ge(w_hi_ready, 1)
            for s in range(2):
                for k in range(3):
                    mm = nc.tensor.matmul(pre[s][k][:], w_hi[:, 0, 0, 0:P], w_hi[:, 0], start=True, stop=True)
            mm.then_inc(banks_marked, 1)
            pe.wait_ge(ident_ready, 1)
            pe.wait_ge(cond_loaded, 16 * 7)
            for c in range(NC):
                mm = nc.tensor.transpose(x_ps[:, c, 0:B], cond_sb[:, c * P:(c + 1) * P], ident[:])
            mm.then_inc(cond_turned, 1)
            pe.wait_ge(cond_t_ready, 1)
            for i, (g, m) in enumerate(TILES):
                if i >= 2:
                    pe.wait_ge(v_ready, i - 1)
                for k in range(NC):
                    mm = nc.tensor.matmul(y_ps[:, 0, 0:B], c_w[:, g, k, m * P:(m + 1) * P], cond_t[:, k],
                                          start=(k == 0), stop=(k == NC - 1)) if i % 2 == 0 else \
                        nc.tensor.matmul(x_ps[:, 0, 0:B], c_w[:, g, k, m * P:(m + 1) * P], cond_t[:, k],
                                         start=(k == 0), stop=(k == NC - 1))
                mm.then_inc(v_summed, 1)
            pe.wait_ge(v_ready, len(TILES))
            turn_x(0, 0, 0, 0)
            turn_x(1, 1, 1, 0)
            pe.wait_ge(w_lo_ready, 1)
            project(0, 0, range(len(TILES)))
            pe.wait_ge(u_loaded, 48)

            def body(pair0, turn, last):
                for q in range(RING):
                    pair, s = pair0 + q, q % 2
                    for j in range(PAIR):
                        t, old = PAIR * pair + j, (j + 1) % 2
                        for k in range(NC):
                            pe.wait_ge(h_ready, NC * t + k + 1)
                            for m in range(NC):
                                mm = times_u(R, s, j, h[:, old, k], k, m)
                                if k == NC - 1:
                                    mm.then_inc(r_summed, 1)
                        for m in range(NC):
                            for k in range(NC):
                                mm = times_u(Z, s, j, h[:, old, k], k, m)
                        mm.then_inc(z_summed, 1)
                        for k in range(NC):
                            pe.wait_ge(rh_ready, NC * t + k + 1)
                            for m in range(NC):
                                if k == 0 and m == 1:
                                    pe.wait_ge(r_ready, NC * t + 2)
                                mm = times_u(H, s, j, rh[:, k], k, m)
                                if k == NC - 1:
                                    mm.then_inc(hh_summed, 1)
                        turn_h(t, old)
                        if j == 0 and not (last and q >= RING - 2):
                            turn_x(pair + 2, s, (q + 2) % RING, turn + (q + 2) // RING)
                        if not (last and q == RING - 1):
                            half = len(TILES) // PAIR
                            project(pair + 1, 1 - s, range(j * half, (j + 1) * half))

            turns(pe, body)
            turn_h(T, (T - 1) % 2)

        @block.scalar
        def _(act):
            def seed(pair, s, tiles):
                for i in tiles:
                    nc.scalar.copy(tile_of(s, i), v[:, i]).then_inc(seeded, 1)

            def take_xt_hi(pair, s):
                act.wait_ge(x_turned, pair + 1)
                if not (isinstance(pair, int) and pair < 2):
                    act.wait_ge(r_summed, NC * PAIR * (pair - 2) + 1)
                nc.scalar.copy(xt_hi[:, s], x_ps[:]).then_inc(xt_hi_ready, 1)

            for g in range(3):
                act.dma_start(c_w[:, g], Cs[g].rearrange("(k p) e -> p k e", p=P)).then_inc(cond_loaded, 16)
            for g in range(3):
                act.dma_start(bias[:, g], bs[g].rearrange("(k p) -> p k", p=P),
                              allow_slow_non_contiguous=True).then_inc(cond_loaded, 16)
            act.wait_ge(cond_turned, 1)
            nc.scalar.copy(cond_t[:], x_ps[:, :, 0:B]).then_inc(cond_t_ready, 1)
            for i, (g, m) in enumerate(TILES):
                act.wait_ge(v_summed, i + 1)
                src = y_ps[:, 0, 0:B] if i % 2 == 0 else x_ps[:, 0, 0:B]
                for j in range(PAIR):
                    op = nc.scalar.activation(v[:, i, j], src, ACT.Identity, bias=bias[:, g, m:m + 1])
                op.then_inc(v_ready, 1)
            act.wait_ge(v_ready, len(TILES))
            act.wait_ge(banks_marked, 1)
            seed(0, 0, range(len(TILES)))
            take_xt_hi(0, 0)
            take_xt_hi(1, 1)

            def body(pair0, turn, last):
                for q in range(RING):
                    pair, s = pair0 + q, q % 2
                    more = not (last and q == RING - 1)
                    for j in range(PAIR):
                        t = PAIR * pair + j
                        for m in range(NC):
                            act.wait_ge(r_summed, NC * t + m + 1)
                            nc.scalar.activation(r[:, m], pre_of(s, R, m)[:, j], ACT.Sigmoid).then_inc(r_ready, 1)
                        act.wait_ge(z_summed, t + 1)
                        nc.scalar.activation(z[:], pre[s][2][:, :, j], ACT.Sigmoid).then_inc(z_ready, 1)
                        if more:
                            seed(pair + 1, 1 - s, (0, 1) if j == 0 else (4, 5))
                        for m in range(NC):
                            act.wait_ge(hh_summed, NC * t + m + 1)
                            nc.scalar.activation(hh[:, m], pre_of(s, H, m)[:, j], ACT.Tanh).then_inc(hh_ready, 1)
                        if more and j == 0:
                            seed(pair + 1, 1 - s, (2, 3))
                        if j == 0 and not (last and q >= RING - 2):
                            take_xt_hi(pair + 2, s)

            turns(act, body)

        @block.vector
        def _(dve):
            def take_xt_lo(pair, s, c):
                dve.wait_ge(xt_hi_ready, pair + 1)
                nc.vector.tensor_tensor(xt_lo[:, s, c], x_ps[:, c], xt_hi[:, s, c].bitcast(F32),
                                        ALU.subtract).then_inc(xt_lo_ready, 1)

            def make_y(t, par, slot, j):
                dve.wait_ge(h_turned, t + 1)
                nc.vector.tensor_tensor(y_ring[:, slot, j], y_ps[:, par], x_ring[:, slot, j],
                                        ALU.add).then_inc(y_ready, 1)

            dve.wait_ge(w_loaded, 48)
            nc.vector.tensor_copy(w_hi[:], w_raw[:]).then_inc(w_hi_ready, 1)
            dve.wait_ge(w_hi_ready, 1)
            nc.vector.tensor_tensor(w_lo[:], w_raw[:], w_hi[:].bitcast(F32), ALU.subtract).then_inc(w_lo_ready, 1)
            take_xt_lo(0, 0, 0)
            take_xt_lo(0, 0, 1)
            take_xt_lo(1, 1, 0)
            take_xt_lo(1, 1, 1)
            dve.wait_ge(x_loaded[RING - 1], 16)
            dve.sem_inc(y_ready, 1)
            for m in range(NC):
                nc.vector.memset(h[:, 1, m], 0.0).then_inc(h_ready, 1)

            def body(pair0, turn, last):
                for q in range(RING):
                    pair, s = pair0 + q, q % 2
                    for j in range(PAIR):
                        t, old, new = PAIR * pair + j, (j + 1) % 2, j
                        for m in range(NC):
                            dve.wait_ge(r_ready, NC * t + m + 1)
                            nc.vector.tensor_tensor(rh[:, m], r[:, m], h[:, old, m], ALU.mult).then_inc(rh_ready, 1)
                        dve.wait_ge(z_ready, t + 1)
                        nc.vector.scalar_tensor_tensor(out=zh[:], in0=z[:], scalar=1.0, in1=h[:, old],
                                                       op0=ALU.subtract, op1=ALU.mult).then_inc(zh_ready, 1)
                        if j == 1 and not (last and q >= RING - 2):
                            take_xt_lo(pair + 2, s, 0)
                            take_xt_lo(pair + 2, s, 1)
                        for m in range(NC):
                            dve.wait_ge(hh_ready, NC * t + m + 1)
                            nc.vector.tensor_tensor(zhh[:, m], z[:, m], hh[:, m], ALU.mult).then_inc(zhh_ready, 1)
                        dve.wait_ge(zh_ready, t + 1)
                        for m in range(NC):
                            dve.wait_ge(zhh_ready, NC * t + m + 1)
                            nc.vector.tensor_tensor(h[:, new, m], zhh[:, m], zh[:, m],
                                                    ALU.subtract).then_inc(h_ready, 1)
                        if j == 1:
                            dve.wait_ge(y_stored[q], 16 * (turn + 1))
                        make_y(t, old, q if j == 1 else (q - 1) % RING, old)

            turns(dve, body)
            make_y(T, 1, RING - 1, 1)


_INS = ["x", "cond_1024"] + [f"L0_cond_{n}" for n in ("W_z", "U_z", "C_z", "b_z", "W_r", "U_r", "C_r", "b_r", "W", "U", "C", "b")]


def kernel(**inputs):
    import numpy as np
    import concourse.bacc as bacc
    from concourse.bass_utils import run_bass_kernel_spmd

    nc = bacc.Bacc("TRN2", target_bir_lowering=False, num_devices=1)
    arrays, args = {}, []
    for name in _INS:
        a = np.ascontiguousarray(inputs[name])
        arrays[f"in_{name}"] = a
        args.append(nc.dram_tensor(f"in_{name}", a.shape, mybir.dt.from_np(a.dtype), kind="ExternalInput").ap())
    out = nc.dram_tensor("out", inputs["x"].shape, F32, kind="ExternalOutput").ap()
    gated_recurrence(nc, *args, out)
    r = run_bass_kernel_spmd(nc, [arrays], core_ids=[0])
    return r.results[0]["out"]
```

```python
from contextlib import ExitStack

import concourse.bass as bass
from concourse import mybir

ALU = mybir.AluOpType
ACT = mybir.ActivationFunctionType
F32 = mybir.dt.float32
F32R = mybir.dt.float32r
F16 = mybir.dt.float16
I32 = mybir.dt.int32

P = 128
NC = 2
PAIR = 2
RING = 4
R, Z, H = 0, 1, 2
TILES = [(R, 0), (H, 0), (R, 1), (H, 1), (Z, 0), (Z, 1)]

PARTS = 3
PRODUCTS = len(TILES) * NC * PARTS
FILLS = [(0, 1, 17), (17, 22, PRODUCTS)]

STATE_BITS = 12
STATE = float(2**STATE_BITS)
U_BITS_MAX = 22
F32_BIAS, F32_MANTISSA, U_TOP = 127, 23, 14


def gated_recurrence(nc, x, cond, Wz, Uz, Cz, bz, Wr, Ur, Cr, br, W, U, C, b, out):
    B, T, D = x.shape
    E = U.shape[1]
    PAIRS = T // PAIR
    TURNS = PAIRS // RING
    assert B == P and D == NC * P and E == NC * P and TURNS * RING * PAIR == T
    Ws, Us, Cs, bs = (Wr, Wz, W), (Ur, Uz, U), (Cr, Cz, C), (br, bz, b)

    with ExitStack() as ctx:
        def sb(name, shape, dt=F32):
            return ctx.enter_context(nc.sbuf_tensor(name, shape, dt))

        def pb(name, shape):
            return ctx.enter_context(nc.psum_tensor(name, shape, F32))

        def sem(name):
            return ctx.enter_context(nc.semaphore(name))

        w_raw = sb("w_raw", [P, 3, NC, E])
        w_hi = sb("w_hi", [P, 3, NC, E], F32R)
        w_lo = sb("w_lo", [P, 3, NC, E], F32R)
        u = sb("u", [P, 3, NC, E])
        u_hi = sb("u_hi", [P, 3, NC, E], F16)
        u_lo = sb("u_lo", [P, 3, NC, E], F16)
        u_max = sb("u_max", [P, 3])
        u_max_t = sb("u_max_t", [3, 1])
        u_max_diag = sb("u_max_diag", [3, 3])
        ones = sb("ones", [3, P])
        exponent = sb("exponent", [P, 3], I32)
        fields = sb("fields", [P, 3, 3], I32)
        scales = sb("scales", [P, 3, 3], I32)
        c_w = sb("c_w", [P, 3, NC, E])
        bias = sb("bias", [P, 3, NC])
        bias_scaled = sb("bias_scaled", [P, 3, NC])
        cond_sb = sb("cond_sb", [B, NC * P])
        cond_t = sb("cond_t", [P, NC, B])
        ident = sb("ident", [P, P])
        blank = sb("blank", [P, 2 * PAIR * B], F16)
        v = sb("v", [P, len(TILES), B])
        x_ring = sb("x_ring", [B, RING, PAIR, D])
        y_ring = sb("y_ring", [B, RING, PAIR, E])
        xt_hi = sb("xt_hi", [P, 2, NC, PAIR * B], F32R)
        xt_lo = sb("xt_lo", [P, 2, NC, PAIR * B], F32R)
        h = sb("h", [P, 2, NC, B])
        h_hi = sb("h_hi", [P, NC, B], F16)
        h_lo = sb("h_lo", [P, NC, B], F16)
        r = sb("r", [P, NC, B])
        z = sb("z", [P, NC, B])
        rh = sb("rh", [P, NC, B])
        rh_hi = sb("rh_hi", [P, NC, B], F16)
        rh_lo = sb("rh_lo", [P, NC, B], F16)
        hh = sb("hh", [P, NC, B])
        zhh = sb("zhh", [P, NC, B])
        zh = sb("zh", [P, NC, B])

        pre = [[pb(f"pre{s}{k}", [P, 2, PAIR, B]) for k in range(3)] for s in range(2)]
        x_ps = pb("x_ps", [P, NC, PAIR * B])
        y_ps = pb("y_ps", [P, 2, E])

        def scale_of(what, g):
            return scales[:, what, g:g + 1].bitcast(F32)

        OF_U, OF_SUM, BACK = range(3)

        def tile_of(s, i):
            return pre[s][i // 2][:, i % 2]

        def pre_of(s, gate, m):
            return tile_of(s, TILES.index((gate, m)))

        u_loaded = [sem(f"u_loaded{g}") for g in range(3)]
        w_loaded = [sem(f"w_loaded{g}") for g in range(3)]
        cond_loaded = sem("cond_loaded")
        x_loaded = [sem(f"x_loaded{k}") for k in range(RING)]
        y_stored = [sem(f"y_stored{k}") for k in range(RING)]
        zeroed = sem("zeroed")
        ident_ready = sem("ident_ready")
        h0_ready = sem("h0_ready")
        w_hi_ready = sem("w_hi_ready")
        w_lo_ready = sem("w_lo_ready")
        banks_marked = sem("banks_marked")
        cond_turned = sem("cond_turned")
        cond_t_ready = sem("cond_t_ready")
        v_summed = sem("v_summed")
        v_ready = sem("v_ready")
        seeded = sem("seeded")
        x_turned = sem("x_turned")
        xt_hi_ready = sem("xt_hi_ready")
        xt_lo_ready = sem("xt_lo_ready")
        r_summed = sem("r_summed")
        z_summed = sem("z_summed")
        hh_summed = sem("hh_summed")
        r_ready = sem("r_ready")
        z_ready = sem("z_ready")
        hh_ready = sem("hh_ready")
        rh_ready = sem("rh_ready")
        rh_hi_ready = sem("rh_hi_ready")
        rh_lo_ready = sem("rh_lo_ready")
        bias_loaded = sem("bias_loaded")
        c_loaded = sem("c_loaded")
        bias_ready = sem("bias_ready")
        zh_ready = sem("zh_ready")
        zhh_ready = sem("zhh_ready")
        h_ready = sem("h_ready")
        blank_ready = sem("blank_ready")
        ones_ready = sem("ones_ready")
        u_split = sem("u_split")
        scales_ready = sem("scales_ready")
        field_ready = sem("field_ready")
        exponent_ready = sem("exponent_ready")
        u_max_spread = sem("u_max_spread")
        u_max_diag_ready = sem("u_max_diag_ready")
        u_max_t_ready = sem("u_max_t_ready")
        u_max_turned = sem("u_max_turned")
        u_max_ready = sem("u_max_ready")
        h_lo_ready = sem("h_lo_ready")
        h_hi_ready = sem("h_hi_ready")
        h_turned = sem("h_turned")
        y_ready = sem("y_ready")

        def turns(eng, body):
            with eng.Fori(0, TURNS - 1) as i:
                body(i * RING, i, False)
            body((TURNS - 1) * RING, TURNS - 1, True)

        block = ctx.enter_context(nc.Block())

        @block.sync
        def _(sp):
            def load_pair(pair, slot):
                sp.dma_start(x_ring[:, slot], x[:, bass.ds(pair * PAIR, PAIR), :]).then_inc(x_loaded[slot], 16)

            for k in range(RING):
                sp.sem_inc(y_stored[k], 16)
            for g in (R, Z, H):
                sp.dma_start(u[:, g], Us[g].rearrange("(k p) e -> p k e", p=P)).then_inc(u_loaded[g], 16)
            sp.dma_start(cond_sb[:], cond).then_inc(cond_loaded, 16)
            load_pair(0, 0)
            for g in (R, H, Z):
                sp.dma_start(w_raw[:, g], Ws[g].rearrange("(k p) e -> p k e", p=P)).then_inc(w_loaded[g], 16)
            for k in range(1, RING):
                load_pair(k, k)

            def body(pair0, turn, last):
                for k in range(RING):
                    sp.wait_ge(y_ready, PAIR * (pair0 + k + 1) + 2)
                    sp.dma_start(out[:, bass.ds((pair0 + k) * PAIR, PAIR), :], y_ring[:, k]).then_inc(y_stored[k], 16)
                    if not last:
                        load_pair(pair0 + k + RING, k)

            turns(sp, body)
            for k in range(RING):
                sp.wait_ge(y_stored[k], 16 * (TURNS + 1))

        @block.gpsimd
        def _(pool):
            nc.gpsimd.memset(ident[:], 0.0).then_inc(zeroed, 1)
            pool.wait_ge(zeroed, 1)
            nc.gpsimd.affine_select(out=ident[:], in_=ident[:], compare_op=ALU.not_equal, fill=1.0, base=0,
                                    pattern=[[-1, P]], channel_multiplier=1).then_inc(ident_ready, 1)
            for g in range(3):
                pool.dma_start(c_w[:, g], Cs[g].rearrange("(k p) e -> p k e", p=P)).then_inc(c_loaded, 16)
            for g in range(3):
                pool.dma_start(bias[:, g], bs[g].rearrange("(k p) -> p k", p=P),
                               allow_slow_non_contiguous=True).then_inc(bias_loaded, 16)

        @block.tensor
        def _(pe):
            def turn_x(pair, s, slot, turn):
                pe.wait_ge(x_loaded[slot], 16 * (turn + 1))
                if not (isinstance(pair, int) and pair == 0):
                    pe.wait_ge(xt_lo_ready, NC * pair)
                for c in range(NC):
                    for j in range(PAIR):
                        mm = nc.tensor.transpose(x_ps[:, c, j * B:(j + 1) * B],
                                                 x_ring[:, slot, j, c * P:(c + 1) * P], ident[:])
                mm.then_inc(x_turned, 1)

            def project(pair, s, first, end):
                for n in range(first, end):
                    i, part, k = n // (NC * PARTS), n // NC % PARTS, n % NC
                    g, m = TILES[i]
                    weights, moving = ((w_hi, xt_hi), (w_lo, xt_hi), (w_hi, xt_lo))[part]
                    if n % (2 * NC * PARTS) == 0:
                        pe.wait_ge(seeded, len(TILES) * pair + i + 2)
                    if n == 0:
                        pe.wait_ge(xt_lo_ready, NC * (pair + 1))
                    nc.tensor.matmul(tile_of(s, i), weights[:, g, k, m * P:(m + 1) * P], moving[:, s, k],
                                     start=False, stop=False, skip_group_check=True)

            def times_u(g, s, j, weights, moving, k, m, last):
                return nc.tensor.matmul(pre_of(s, g, m)[:, j], weights[:, g, k, m * P:(m + 1) * P], moving[:, k],
                                        start=False, stop=last, skip_group_check=True)

            def turn_h(t, par):
                pe.wait_ge(y_ready, t + 1)
                pe.wait_ge(h_ready, NC * (t + 1))
                for c in range(NC):
                    mm = nc.tensor.transpose(y_ps[:, par, c * P:(c + 1) * P], h[:, par, c], ident[:])
                mm.then_inc(h_turned, 1)

            pe.wait_ge(ident_ready, 1)
            pe.wait_ge(cond_loaded, 16)
            for c in range(NC):
                mm = nc.tensor.transpose(y_ps[:, 0, c * P:(c + 1) * P], cond_sb[:, c * P:(c + 1) * P], ident[:])
            mm.then_inc(cond_turned, 1)
            pe.wait_ge(u_max_ready, 3)
            nc.tensor.transpose(pre[0][0][0:3, 0, 0], u_max[:], ident[:]).then_inc(u_max_turned, 1)
            pe.wait_ge(u_max_diag_ready, 1)
            pe.wait_ge(ones_ready, 1)
            nc.tensor.matmul(pre[0][0][:, 0, 0, 0:3], ones[:], u_max_diag[:], start=True,
                             stop=True).then_inc(u_max_spread, 1)
            turn_x(0, 0, 0, 0)
            pe.wait_ge(cond_t_ready, 1)
            pe.wait_ge(c_loaded, 48)
            for i, (g, m) in enumerate(TILES):
                for k in range(NC):
                    mm = nc.tensor.matmul(pre[1][i // 4][:, i // 2 % 2, i % 2], c_w[:, g, k, m * P:(m + 1) * P],
                                          cond_t[:, k], start=(k == 0), stop=(k == NC - 1))
            mm.then_inc(v_summed, 1)
            pe.wait_ge(blank_ready, 1)
            pe.wait_ge(exponent_ready, 1)
            for s in range(2):
                if s == 1:
                    pe.wait_ge(v_ready, len(TILES))
                for k in range(3):
                    mm = nc.tensor.matmul(pre[s][k][:], blank[:, 0:P], blank[:], start=True, stop=True)
                mm.then_inc(banks_marked, 1)
            turn_x(1, 1, 1, 0)
            pe.wait_ge(w_lo_ready, 3)
            project(0, 0, 0, PRODUCTS)
            pe.wait_ge(u_split, 6)

            def body(pair0, turn, last):
                for q in range(RING):
                    pair, s = pair0 + q, q % 2
                    more = not (last and q == RING - 1)
                    for j in range(PAIR):
                        t, old = PAIR * pair + j, (j + 1) % 2
                        for g in (R, Z):
                            for k in range(NC):
                                if g == R:
                                    pe.wait_ge(h_hi_ready, NC * t + k + 1)
                                for m in range(NC):
                                    times_u(g, s, j, u_hi, h_hi, k, m, False)
                                    times_u(g, s, j, u_lo, h_hi, k, m, False)
                            for k in range(NC):
                                if g == R:
                                    pe.wait_ge(h_lo_ready, NC * t + k + 1)
                                for m in range(NC):
                                    mm = times_u(g, s, j, u_hi, h_lo, k, m, k == NC - 1)
                                    if g == R and k == NC - 1:
                                        mm.then_inc(r_summed, 1)
                        mm.then_inc(z_summed, 1)
                        n0, n1, n2 = FILLS[j]
                        if j == 0 and not (last and q >= RING - 2):
                            turn_x(pair + 2, s, (q + 2) % RING, turn + (q + 2) // RING)
                        if more:
                            project(pair + 1, 1 - s, n0, n1)
                        for k in range(NC):
                            pe.wait_ge(rh_hi_ready, NC * t + k + 1)
                            for m in range(NC):
                                if k == 0 and m == 1:
                                    pe.wait_ge(r_ready, NC * t + 2)
                                times_u(H, s, j, u_hi, rh_hi, k, m, False)
                                times_u(H, s, j, u_lo, rh_hi, k, m, False)
                        for k in range(NC):
                            pe.wait_ge(rh_lo_ready, NC * t + k + 1)
                            for m in range(NC):
                                mm = times_u(H, s, j, u_hi, rh_lo, k, m, k == NC - 1)
                                if k == NC - 1:
                                    mm.then_inc(hh_summed, 1)
                        turn_h(t, old)
                        if more:
                            project(pair + 1, 1 - s, n1, n2)

            turns(pe, body)
            turn_h(T, (T - 1) % 2)

        @block.scalar
        def _(act):
            def seed(pair, s, tiles):
                for i in tiles:
                    nc.scalar.copy(tile_of(s, i), v[:, i:i + 1].to_broadcast([P, PAIR, B])).then_inc(seeded, 1)

            def take_xt_hi(pair, s):
                act.wait_ge(x_turned, pair + 1)
                if not (isinstance(pair, int) and pair < 2):
                    act.wait_ge(r_summed, NC * PAIR * (pair - 2) + 1)
                nc.scalar.copy(xt_hi[:, s], x_ps[:]).then_inc(xt_hi_ready, 1)

            nc.scalar.preload_act_table(ACT.Sigmoid)
            act.wait_ge(cond_turned, 1)
            nc.scalar.copy(cond_t[:], y_ps[:, 0].rearrange("p (c b) -> p c b", c=NC)).then_inc(cond_t_ready, 1)
            take_xt_hi(0, 0)
            act.wait_ge(scales_ready, 1)
            for n, g in enumerate((R, H, Z)):
                act.wait_ge(w_loaded[g], 16)
                nc.scalar.activation(w_hi[:, g], w_raw[:, g], ACT.Copy, scale=scale_of(OF_SUM, g)).then_inc(w_hi_ready, 1)
                if n == 0:
                    act.wait_ge(v_summed, 1)
                    act.wait_ge(bias_ready, 3)
                for i in (2 * n, 2 * n + 1):
                    vg, m = TILES[i]
                    nc.scalar.activation(v[:, i], pre[1][i // 4][:, i // 2 % 2, i % 2], ACT.Identity,
                                         bias=bias_scaled[:, vg, m:m + 1], scale=scale_of(OF_SUM, vg)).then_inc(v_ready, 1)
            act.wait_ge(v_ready, len(TILES))
            act.wait_ge(banks_marked, 1)
            seed(0, 0, range(len(TILES)))
            act.wait_ge(banks_marked, 2)
            seed(1, 1, (0, 1))
            take_xt_hi(1, 1)

            def body(pair0, turn, last):
                for q in range(RING):
                    pair, s = pair0 + q, q % 2
                    more = not (last and q == RING - 1)
                    for j in range(PAIR):
                        t = PAIR * pair + j
                        for m in range(NC):
                            act.wait_ge(r_summed, NC * t + m + 1)
                            nc.scalar.activation(r[:, m], pre_of(s, R, m)[:, j], ACT.Sigmoid,
                                                 scale=scale_of(BACK, R)).then_inc(r_ready, 1)
                        for m in range(NC):
                            act.wait_ge(rh_ready, NC * t + m + 1)
                            nc.scalar.copy(rh_hi[:, m], rh[:, m]).then_inc(rh_hi_ready, 1)
                        act.wait_ge(z_summed, t + 1)
                        nc.scalar.activation(z[:], pre[s][2][:, :, j], ACT.Sigmoid,
                                             scale=scale_of(BACK, Z)).then_inc(z_ready, 1)
                        if more:
                            seed(pair + 1, 1 - s, (2,) if j == 0 else (5,))
                        for m in range(NC):
                            act.wait_ge(hh_summed, NC * t + m + 1)
                            nc.scalar.activation(hh[:, m], pre_of(s, H, m)[:, j], ACT.Tanh,
                                                 scale=scale_of(BACK, H)).then_inc(hh_ready, 1)
                        seed_next = (lambda i: seed(pair + 1, 1 - s, (i + 3,))) if j == 0 else \
                                    (lambda i: seed(pair + 2, s, (i,)))
                        seeds = more if j == 0 else not (last and q >= RING - 2)
                        if seeds:
                            if j == 1:
                                act.wait_ge(hh_ready, NC * (t + 1))
                            seed_next(0)
                        for m in range(NC):
                            act.wait_ge(h_ready, NC * (t + 1) + m + 1)
                            nc.scalar.copy(h_hi[:, m], h[:, j, m]).then_inc(h_hi_ready, 1)
                        if seeds:
                            seed_next(1)
                        if j == 0 and not (last and q >= RING - 2):
                            take_xt_hi(pair + 2, s)

            turns(act, body)

        @block.vector
        def _(dve):
            def take_xt_lo(pair, s, c):
                dve.wait_ge(xt_hi_ready, pair + 1)
                nc.vector.tensor_tensor(xt_lo[:, s, c], x_ps[:, c], xt_hi[:, s, c].bitcast(F32),
                                        ALU.subtract).then_inc(xt_lo_ready, 1)

            def make_y(t, par, slot, j):
                dve.wait_ge(h_turned, t + 1)
                nc.vector.scalar_tensor_tensor(out=y_ring[:, slot, j], in0=y_ps[:, par], scalar=1.0 / STATE,
                                               in1=x_ring[:, slot, j], op0=ALU.mult, op1=ALU.add).then_inc(y_ready, 1)

            nc.vector.memset(blank[:], 0.0).then_inc(blank_ready, 1)
            nc.vector.memset(ones[:], 1.0).then_inc(ones_ready, 1)
            for g in (R, Z, H):
                dve.wait_ge(u_loaded[g], 16)
                nc.vector.tensor_reduce(u_max[:, g:g + 1], u[:, g], mybir.AxisListType.XY, ALU.max,
                                        apply_absolute_value=True).then_inc(u_max_ready, 1)
            dve.wait_ge(u_max_turned, 1)
            nc.vector.tensor_reduce(u_max_t[:], pre[0][0][0:3, 0, 0], mybir.AxisListType.X,
                                    ALU.max).then_inc(u_max_t_ready, 1)
            dve.wait_ge(u_max_t_ready, 1)
            nc.vector.tensor_scalar(u_max_diag[:], ident[0:3, 0:3], u_max_t[:, 0:1], None,
                                    ALU.mult).then_inc(u_max_diag_ready, 1)
            dve.wait_ge(u_max_spread, 1)
            nc.vector.tensor_single_scalar(exponent[:], pre[0][0][:, 0, 0, 0:3].bitcast(I32), F32_MANTISSA,
                                           ALU.logical_shift_right).then_inc(exponent_ready, 1)
            dve.wait_ge(exponent_ready, 1)
            nc.vector.tensor_scalar(fields[:, OF_U], exponent[:], -1, U_TOP + 2 * F32_BIAS, ALU.mult,
                                    ALU.add).then_inc(field_ready, 1)
            dve.wait_ge(field_ready, 1)
            nc.vector.tensor_single_scalar(fields[:, OF_U], fields[:, OF_U], F32_BIAS + U_BITS_MAX,
                                           ALU.min).then_inc(field_ready, 1)
            dve.wait_ge(field_ready, 2)
            nc.vector.tensor_single_scalar(fields[:, OF_SUM], fields[:, OF_U], STATE_BITS,
                                           ALU.add).then_inc(field_ready, 1)
            nc.vector.tensor_scalar(fields[:, BACK], fields[:, OF_U], -1, 2 * F32_BIAS - STATE_BITS, ALU.mult,
                                    ALU.add).then_inc(field_ready, 1)
            dve.wait_ge(field_ready, 4)
            nc.vector.tensor_single_scalar(scales[:], fields[:], F32_MANTISSA,
                                           ALU.logical_shift_left).then_inc(scales_ready, 1)
            dve.wait_ge(scales_ready, 1)
            dve.wait_ge(bias_loaded, 48)
            for g in range(3):
                nc.vector.tensor_scalar(bias_scaled[:, g], bias[:, g], scale_of(OF_SUM, g), None,
                                        ALU.mult).then_inc(bias_ready, 1)
            take_xt_lo(0, 0, 0)
            take_xt_lo(0, 0, 1)
            for n, g in enumerate((R, H, Z)):
                dve.wait_ge(w_hi_ready, n + 1)
                nc.vector.scalar_tensor_tensor(out=w_lo[:, g], in0=w_raw[:, g], scalar=scale_of(OF_SUM, g),
                                               in1=w_hi[:, g].bitcast(F32), op0=ALU.mult,
                                               op1=ALU.subtract).then_inc(w_lo_ready, 1)
            for g in range(3):
                nc.vector.tensor_scalar(u_hi[:, g], u[:, g], scale_of(OF_U, g), None, ALU.mult).then_inc(u_split, 1)
            for g in range(3):
                dve.wait_ge(u_split, g + 1)
                nc.vector.scalar_tensor_tensor(out=u_lo[:, g], in0=u[:, g], scalar=scale_of(OF_U, g),
                                               in1=u_hi[:, g], op0=ALU.mult, op1=ALU.subtract).then_inc(u_split, 1)
            take_xt_lo(1, 1, 0)
            take_xt_lo(1, 1, 1)
            dve.wait_ge(x_loaded[RING - 1], 16)
            dve.sem_inc(y_ready, 1)
            for m in range(NC):
                nc.vector.memset(h[:, 1, m], 0.0).then_inc(h_ready, 1)
                nc.vector.memset(h_hi[:, m], 0.0).then_inc(h_hi_ready, 1)
                nc.vector.memset(h_lo[:, m], 0.0).then_inc(h_lo_ready, 1)

            def body(pair0, turn, last):
                for q in range(RING):
                    pair, s = pair0 + q, q % 2
                    for j in range(PAIR):
                        t, old, new = PAIR * pair + j, (j + 1) % 2, j
                        for m in range(NC):
                            dve.wait_ge(r_ready, NC * t + m + 1)
                            nc.vector.tensor_tensor(rh[:, m], r[:, m], h[:, old, m], ALU.mult).then_inc(rh_ready, 1)
                        for m in range(NC):
                            dve.wait_ge(rh_hi_ready, NC * t + m + 1)
                            nc.vector.tensor_tensor(rh_lo[:, m], rh[:, m], rh_hi[:, m], ALU.subtract).then_inc(rh_lo_ready, 1)
                        dve.wait_ge(z_ready, t + 1)
                        nc.vector.scalar_tensor_tensor(out=zh[:], in0=z[:], scalar=1.0, in1=h[:, old],
                                                       op0=ALU.subtract, op1=ALU.mult).then_inc(zh_ready, 1)
                        if j == 1 and not (last and q >= RING - 2):
                            take_xt_lo(pair + 2, s, 0)
                            take_xt_lo(pair + 2, s, 1)
                        for m in range(NC):
                            dve.wait_ge(hh_ready, NC * t + m + 1)
                            nc.vector.scalar_tensor_tensor(out=zhh[:, m], in0=z[:, m], scalar=STATE, in1=hh[:, m],
                                                           op0=ALU.mult, op1=ALU.mult).then_inc(zhh_ready, 1)
                        dve.wait_ge(zh_ready, t + 1)
                        for m in range(NC):
                            dve.wait_ge(zhh_ready, NC * t + m + 1)
                            nc.vector.tensor_tensor(h[:, new, m], zhh[:, m], zh[:, m],
                                                    ALU.subtract).then_inc(h_ready, 1)
                        for m in range(NC):
                            dve.wait_ge(h_hi_ready, NC * (t + 1) + m + 1)
                            nc.vector.tensor_tensor(h_lo[:, m], h[:, new, m], h_hi[:, m],
                                                    ALU.subtract).then_inc(h_lo_ready, 1)
                        if j == 1:
                            dve.wait_ge(y_stored[q], 16 * (turn + 1))
                        make_y(t, old, q if j == 1 else (q - 1) % RING, old)

            turns(dve, body)
            make_y(T, 1, RING - 1, 1)


_INS = ["x", "cond_1024"] + [f"L0_cond_{n}" for n in ("W_z", "U_z", "C_z", "b_z", "W_r", "U_r", "C_r", "b_r", "W", "U", "C", "b")]


def kernel(**inputs):
    import numpy as np
    import concourse.bacc as bacc
    from concourse.bass_utils import run_bass_kernel_spmd

    nc = bacc.Bacc("TRN2", target_bir_lowering=False, num_devices=1)
    arrays, args = {}, []
    for name in _INS:
        a = np.ascontiguousarray(inputs[name])
        arrays[f"in_{name}"] = a
        args.append(nc.dram_tensor(f"in_{name}", a.shape, mybir.dt.from_np(a.dtype), kind="ExternalInput").ap())
    out = nc.dram_tensor("out", inputs["x"].shape, F32, kind="ExternalOutput").ap()
    gated_recurrence(nc, *args, out)
    r = run_bass_kernel_spmd(nc, [arrays], core_ids=[0])
    return r.results[0]["out"]
```

```python
from contextlib import ExitStack

import concourse.bass as bass
from concourse import mybir

ALU = mybir.AluOpType
ACT = mybir.ActivationFunctionType
F32 = mybir.dt.float32
F32R = mybir.dt.float32r
F16 = mybir.dt.float16
I32 = mybir.dt.int32

P = 128
NC = 2
PAIR = 2
RING = 4
R, Z, H = 0, 1, 2
TILES = [(R, 0), (H, 0), (R, 1), (H, 1), (Z, 0), (Z, 1)]

PARTS = 3
PRODUCTS = len(TILES) * NC * PARTS
LATE = PRODUCTS - 4
FILLS = 13, 17
V_BANKS = (R, H, Z)
START = (0, 2, 1, 3, 4, 5)
WARMING = 11

STATE_BITS = 12
STATE = float(2**STATE_BITS)
U_BITS_MAX = 22
F32_BIAS, F32_MANTISSA, U_TOP = 127, 23, 14


def gated_recurrence(nc, x, cond, Wz, Uz, Cz, bz, Wr, Ur, Cr, br, W, U, C, b, out):
    B, T, D = x.shape
    E = U.shape[1]
    PAIRS = T // PAIR
    TURNS = PAIRS // RING
    assert B == P and D == NC * P and E == NC * P and TURNS * RING * PAIR == T
    Ws, Us, Cs, bs = (Wr, Wz, W), (Ur, Uz, U), (Cr, Cz, C), (br, bz, b)

    with ExitStack() as ctx:
        def sb(name, shape, dt=F32):
            return ctx.enter_context(nc.sbuf_tensor(name, shape, dt))

        def pb(name, shape):
            return ctx.enter_context(nc.psum_tensor(name, shape, F32))

        def sem(name):
            return ctx.enter_context(nc.semaphore(name))

        w_raw = sb("w_raw", [P, 3, NC, E])
        w_hi = sb("w_hi", [P, 3, NC, E], F32R)
        w_lo = sb("w_lo", [P, 3, NC, E], F32R)
        u = sb("u", [P, 3, NC, E])
        u_hi = sb("u_hi", [P, 3, NC, E], F16)
        u_lo = sb("u_lo", [P, 3, NC, E], F16)
        u_max = sb("u_max", [P, 3])
        u_max_t = sb("u_max_t", [3, 1])
        u_max_diag = sb("u_max_diag", [3, 3])
        ones = sb("ones", [3, P])
        exponent = sb("exponent", [P, 3], I32)
        minus_exponent = sb("minus_exponent", [P, 3], I32)
        fields = sb("fields", [P, 3, 3], I32)
        scales = sb("scales", [P, 3, 3], I32)
        c_w = sb("c_w", [P, 3, NC, E])
        bias = sb("bias", [3 * NC, P])
        bias_scaled = sb("bias_scaled", [P, 3, NC])
        cond_sb = sb("cond_sb", [B, NC * P])
        cond_t = sb("cond_t", [P, NC, B])
        ident = sb("ident", [P, P])
        blank = sb("blank", [P, 2 * PAIR * B], F16)
        v = sb("v", [P, len(TILES), B])
        x_ring = sb("x_ring", [B, RING, PAIR, D])
        y_ring = sb("y_ring", [B, RING, PAIR, E])
        xt_hi = sb("xt_hi", [P, 2, NC, PAIR * B], F32R)
        xt_lo = sb("xt_lo", [P, 2, NC, PAIR * B], F32R)
        h = sb("h", [P, 2, NC, B])
        h_hi = sb("h_hi", [P, NC, B], F16)
        h_lo = sb("h_lo", [P, NC, B], F16)
        r = sb("r", [P, NC, B])
        z = sb("z", [P, NC, B])
        rh = sb("rh", [P, NC, B])
        rh_hi = sb("rh_hi", [P, NC, B], F16)
        rh_lo = sb("rh_lo", [P, NC, B], F16)
        hh = sb("hh", [P, NC, B])
        zhh = sb("zhh", [P, NC, B])
        zh = sb("zh", [P, NC, B])

        pre = [[pb(f"pre{s}{k}", [P, 2, PAIR, B]) for k in range(3)] for s in range(2)]
        x_ps = pb("x_ps", [P, NC, PAIR * B])
        y_ps = pb("y_ps", [P, 2, E])

        def scale_of(what, g):
            return scales[:, what, g:g + 1].bitcast(F32)

        OF_U, OF_SUM, BACK = range(3)

        def v_sum(g):
            return pre[1][V_BANKS.index(g)][:, :, 0]

        def tile_of(s, i):
            return pre[s][i // 2][:, i % 2]

        def pre_of(s, gate, m):
            return tile_of(s, TILES.index((gate, m)))

        u_loaded = [sem(f"u_loaded{g}") for g in range(3)]
        w_loaded = [sem(f"w_loaded{g}") for g in range(3)]
        c_loaded = [sem(f"c_loaded{g}") for g in range(3)]
        bias_loaded = sem("bias_loaded")
        cond_loaded = sem("cond_loaded")
        x_loaded = [sem(f"x_loaded{k}") for k in range(RING)]
        y_stored = [sem(f"y_stored{k}") for k in range(RING)]
        zeroed = sem("zeroed")
        ident_ready = sem("ident_ready")
        blank_ready = sem("blank_ready")
        ones_ready = sem("ones_ready")
        banks_marked = sem("banks_marked")
        u_max_ready = sem("u_max_ready")
        u_max_turned = sem("u_max_turned")
        u_max_t_ready = sem("u_max_t_ready")
        u_max_diag_ready = sem("u_max_diag_ready")
        u_max_spread = sem("u_max_spread")
        exponent_ready = sem("exponent_ready")
        field_ready = sem("field_ready")
        scales_ready = sem("scales_ready")
        w_hi_ready = [sem(f"w_hi_ready{g}") for g in range(3)]
        w_lo_ready = [sem(f"w_lo_ready{g}") for g in range(3)]
        u_hi_ready = [sem(f"u_hi_ready{g}") for g in range(3)]
        u_lo_ready = sem("u_lo_ready")
        cond_turned = sem("cond_turned")
        cond_t_ready = sem("cond_t_ready")
        bias_turned = sem("bias_turned")
        bias_ready = sem("bias_ready")
        v_summed = sem("v_summed")
        v_ready = sem("v_ready")
        v_z_ready = sem("v_z_ready")
        seeded = sem("seeded")
        x_turned = sem("x_turned")
        xt_hi_ready = sem("xt_hi_ready")
        xt_lo_ready = sem("xt_lo_ready")
        r_summed = sem("r_summed")
        r_ready = sem("r_ready")
        rh_ready = sem("rh_ready")
        rh_hi_ready = sem("rh_hi_ready")
        rh_lo_ready = sem("rh_lo_ready")
        z_summed = sem("z_summed")
        z_ready = sem("z_ready")
        zh_ready = sem("zh_ready")
        hh_summed = sem("hh_summed")
        hh_ready = sem("hh_ready")
        zhh_ready = sem("zhh_ready")
        h_ready = sem("h_ready")
        h_hi_ready = sem("h_hi_ready")
        h_lo_ready = sem("h_lo_ready")
        h_turned = sem("h_turned")
        y_ready = sem("y_ready")

        def turns(eng, body):
            with eng.Fori(0, TURNS - 1) as i:
                body(i * RING, i, False)
            body((TURNS - 1) * RING, TURNS - 1, True)

        block = ctx.enter_context(nc.Block())

        @block.sync
        def _(sp):
            def load_pair(pair, slot):
                sp.dma_start(x_ring[:, slot], x[:, bass.ds(pair * PAIR, PAIR), :]).then_inc(x_loaded[slot], 16)

            def load_matrix(place, g, matrices, loaded):
                sp.dma_start(place[:, g], matrices[g].rearrange("(k p) e -> p k e", p=P)).then_inc(loaded[g], 16)

            for k in range(RING):
                sp.sem_inc(y_stored[k], 16)

            for g in (R, Z, H):
                load_matrix(u, g, Us, u_loaded)
            sp.dma_start(cond_sb[:], cond).then_inc(cond_loaded, 16)
            load_matrix(c_w, R, Cs, c_loaded)
            load_pair(0, 0)
            load_matrix(c_w, H, Cs, c_loaded)
            load_matrix(w_raw, R, Ws, w_loaded)
            load_matrix(c_w, Z, Cs, c_loaded)
            load_matrix(w_raw, H, Ws, w_loaded)
            load_matrix(w_raw, Z, Ws, w_loaded)
            for k in range(1, RING):
                load_pair(k, k)

            def body(pair0, turn, last):
                for k in range(RING):
                    if last and k == RING - 1:
                        for j in range(PAIR):
                            sp.wait_ge(y_ready, T + j + 1)
                            sp.dma_start(out[:, T - PAIR + j, :], y_ring[:, k, j]).then_inc(y_stored[k], 16)
                        break
                    sp.wait_ge(y_ready, PAIR * (pair0 + k + 1) + 2)
                    sp.dma_start(out[:, bass.ds((pair0 + k) * PAIR, PAIR), :], y_ring[:, k]).then_inc(y_stored[k], 16)
                    if not last:
                        load_pair(pair0 + k + RING, k)

            turns(sp, body)
            for k in range(RING):
                sp.wait_ge(y_stored[k], 16 * (TURNS + 1 + (k == RING - 1)))

        @block.gpsimd
        def _(pool):
            nc.gpsimd.memset(ident[:], 0.0).then_inc(zeroed, 1)
            pool.wait_ge(zeroed, 1)
            nc.gpsimd.affine_select(out=ident[:], in_=ident[:], compare_op=ALU.not_equal, fill=1.0, base=0,
                                    pattern=[[-1, P]], channel_multiplier=1).then_inc(ident_ready, 1)
            for g in range(3):
                pool.dma_start(bias[NC * g:NC * (g + 1), :], bs[g].rearrange("(k p) -> k p", p=P)).then_inc(bias_loaded, 16)
            pool.wait_ge(scales_ready, 1)
            for g in (R, Z):
                nc.gpsimd.tensor_scalar(u_hi[:, g], u[:, g], scale_of(OF_U, g), None,
                                        ALU.mult).then_inc(u_hi_ready[g], 1)

        @block.tensor
        def _(pe):
            def turn_x(pair, s, slot, turn):
                pe.wait_ge(x_loaded[slot], 16 * (turn + 1))
                if not (isinstance(pair, int) and pair == 0):
                    pe.wait_ge(xt_lo_ready, NC * pair)
                for c in range(NC):
                    for j in range(PAIR):
                        mm = nc.tensor.transpose(x_ps[:, c, j * B:(j + 1) * B],
                                                 x_ring[:, slot, j, c * P:(c + 1) * P], ident[:])
                mm.then_inc(x_turned, 1)

            def project(pair, s, first, end):
                at_start = isinstance(pair, int) and pair == 0
                for n in range(first, end):
                    i, part, k = n // (NC * PARTS), n // NC % PARTS, n % NC
                    if at_start:
                        i = START[i]
                    g, m = TILES[i]
                    weights, moving = ((w_hi, xt_hi), (w_lo, xt_hi), (w_hi, xt_lo))[part]
                    if at_start and k == 0:
                        if part == 0:
                            pe.wait_ge(seeded, i // 2 * 2 + 2)
                            pe.wait_ge(xt_hi_ready, 1)
                            pe.wait_ge(w_hi_ready[g], 1)
                        elif part == 1:
                            pe.wait_ge(w_lo_ready[g], 1)
                        else:
                            pe.wait_ge(xt_lo_ready, NC)
                    if not at_start and n % (2 * NC * PARTS) == 0:
                        pe.wait_ge(seeded, len(TILES) * pair + i + 2)
                    if not at_start and n == 0:
                        pe.wait_ge(xt_lo_ready, NC * (pair + 1))
                    mm = nc.tensor.matmul(tile_of(s, i), weights[:, g, k, m * P:(m + 1) * P], moving[:, s, k],
                                          start=False, stop=False, skip_group_check=True)
                return mm

            def times_u(g, s, j, weights, moving, k, m, last):
                return nc.tensor.matmul(pre_of(s, g, m)[:, j], weights[:, g, k, m * P:(m + 1) * P], moving[:, k],
                                        start=False, stop=last, skip_group_check=True)

            def turn_h(t, par):
                pe.wait_ge(y_ready, t + 1)
                pe.wait_ge(h_ready, NC * (t + 1))
                for c in range(NC):
                    mm = nc.tensor.transpose(y_ps[:, par, c * P:(c + 1) * P], h[:, par, c], ident[:])
                mm.then_inc(h_turned, 1)

            def sum_v(g):
                pe.wait_ge(c_loaded[g], 16)
                for m in range(NC):
                    for k in range(NC):
                        mm = nc.tensor.matmul(v_sum(g)[:, m], c_w[:, g, k, m * P:(m + 1) * P], cond_t[:, k],
                                              start=False, stop=(k == NC - 1), skip_group_check=True)
                mm.then_inc(v_summed, 1)

            pe.wait_ge(blank_ready, 1)
            for n in range(WARMING):
                mm = nc.tensor.matmul(pre[n // 3 % 2][n % 3][:], blank[:, 0:P], blank[:], start=True, stop=True)
            mm.then_inc(banks_marked, 1)
            pe.wait_ge(ident_ready, 1)
            pe.wait_ge(u_max_ready, 3)
            nc.tensor.transpose(y_ps[0:3, 0, 0:P], u_max[:], ident[:]).then_inc(u_max_turned, 1)
            pe.wait_ge(cond_loaded, 16)
            for c in range(NC):
                mm = nc.tensor.transpose(x_ps[:, 0, c * B:(c + 1) * B], cond_sb[:, c * P:(c + 1) * P], ident[:])
            mm.then_inc(cond_turned, 1)
            pe.wait_ge(u_max_diag_ready, 1)
            pe.wait_ge(ones_ready, 1)
            nc.tensor.matmul(y_ps[:, 0, 0:3], ones[:], u_max_diag[:], start=True, stop=True).then_inc(u_max_spread, 1)
            pe.wait_ge(cond_t_ready, 1)
            turn_x(0, 0, 0, 0)
            sum_v(R)
            pe.wait_ge(exponent_ready, 1)
            pe.wait_ge(bias_loaded, 48)
            nc.tensor.transpose(y_ps[:, 1, 0:3 * NC], bias[:], ident[0:3 * NC, 0:3 * NC]).then_inc(bias_turned, 1)
            sum_v(H)
            sum_v(Z)
            project(0, 0, 0, PRODUCTS // 3)
            turn_x(1, 1, 1, 0)
            project(0, 0, PRODUCTS // 3, LATE)
            pe.wait_ge(u_hi_ready[R], 1)
            pe.wait_ge(u_hi_ready[Z], 1)
            pe.wait_ge(u_lo_ready, 2)

            def body(pair0, turn, last):
                for q in range(RING):
                    pair, s = pair0 + q, q % 2
                    more = not (last and q == RING - 1)
                    for j in range(PAIR):
                        t, old = PAIR * pair + j, (j + 1) % 2
                        for g in (R, Z):
                            for k in range(NC):
                                if g == R:
                                    pe.wait_ge(h_hi_ready, NC * t + k + 1)
                                for m in range(NC):
                                    times_u(g, s, j, u_hi, h_hi, k, m, False)
                                    times_u(g, s, j, u_lo, h_hi, k, m, False)
                            for k in range(NC):
                                if g == R:
                                    pe.wait_ge(h_lo_ready, NC * t + k + 1)
                                for m in range(NC):
                                    mm = times_u(g, s, j, u_hi, h_lo, k, m, k == NC - 1)
                                    if g == R and k == NC - 1:
                                        mm.then_inc(r_summed, 1)
                        if j == 0:
                            turn_h(t, old)
                            mm = project(pair, s, LATE, PRODUCTS)
                        mm.then_inc(z_summed, 1)
                        if j == 1:
                            turn_h(t, old)
                            if more:
                                project(pair + 1, 1 - s, FILLS[0], FILLS[1])
                        for k in range(NC):
                            pe.wait_ge(rh_hi_ready, NC * t + k + 1)
                            for m in range(NC):
                                if k == 0 and m == 1:
                                    pe.wait_ge(r_ready, NC * t + 2)
                                times_u(H, s, j, u_hi, rh_hi, k, m, False)
                                times_u(H, s, j, u_lo, rh_hi, k, m, False)
                        for k in range(NC):
                            pe.wait_ge(rh_lo_ready, NC * t + k + 1)
                            for m in range(NC):
                                mm = times_u(H, s, j, u_hi, rh_lo, k, m, k == NC - 1)
                                if k == NC - 1:
                                    mm.then_inc(hh_summed, 1)
                        if j == 0 and not (last and q >= RING - 2):
                            turn_x(pair + 2, s, (q + 2) % RING, turn + (q + 2) // RING)
                        if more:
                            if j == 0:
                                project(pair + 1, 1 - s, 0, FILLS[0])
                            else:
                                project(pair + 1, 1 - s, FILLS[1], LATE)

            turns(pe, body)
            turn_h(T, (T - 1) % 2)

        @block.scalar
        def _(act):
            def seed(pair, s, tiles):
                for i in tiles:
                    nc.scalar.copy(tile_of(s, i), v[:, i:i + 1].to_broadcast([P, PAIR, B])).then_inc(seeded, 1)

            def take_xt_hi(pair, s):
                act.wait_ge(x_turned, pair + 1)
                if not (isinstance(pair, int) and pair < 2):
                    act.wait_ge(z_summed, PAIR * (pair - 2) + 1)
                nc.scalar.copy(xt_hi[:, s], x_ps[:]).then_inc(xt_hi_ready, 1)

            nc.scalar.preload_act_table(ACT.Sigmoid)
            act.wait_ge(cond_turned, 1)
            nc.scalar.copy(cond_t[:], x_ps[:, 0].rearrange("p (c b) -> p c b", c=NC)).then_inc(cond_t_ready, 1)
            take_xt_hi(0, 0)
            act.wait_ge(banks_marked, 1)
            act.wait_ge(scales_ready, 1)
            act.wait_ge(bias_ready, 1)

            def add_bias(place, g, source, m):
                return nc.scalar.activation(place, source, ACT.Identity, bias=bias_scaled[:, g, m:m + 1],
                                            scale=scale_of(OF_SUM, g))

            for bank in range(3):
                for i in (2 * bank, 2 * bank + 1):
                    g, m = TILES[i]
                    act.wait_ge(v_summed, 1 + V_BANKS.index(g))
                    add_bias(tile_of(0, i), g, v_sum(g)[:, m:m + 1].to_broadcast([P, PAIR, B]), m).then_inc(seeded, 1)
                if bank == 1:
                    act.wait_ge(w_loaded[Z], 16)
                    nc.scalar.activation(w_hi[:, Z], w_raw[:, Z], ACT.Copy,
                                         scale=scale_of(OF_SUM, Z)).then_inc(w_hi_ready[Z], 1)
            for i in (0, 2, 1, 3):
                g, m = TILES[i]
                add_bias(v[:, i], g, v_sum(g)[:, m], m).then_inc(v_ready, 1)
            take_xt_hi(1, 1)
            act.wait_ge(v_ready, 4)
            seed(1, 1, (0, 1))
            act.wait_ge(v_z_ready, NC)

            def body(pair0, turn, last):
                for q in range(RING):
                    pair, s = pair0 + q, q % 2
                    more = not (last and q == RING - 1)
                    for j in range(PAIR):
                        t = PAIR * pair + j
                        for m in range(NC):
                            act.wait_ge(r_summed, NC * t + m + 1)
                            nc.scalar.activation(r[:, m], pre_of(s, R, m)[:, j], ACT.Sigmoid,
                                                 scale=scale_of(BACK, R)).then_inc(r_ready, 1)
                        for m in range(NC):
                            act.wait_ge(rh_ready, NC * t + m + 1)
                            nc.scalar.copy(rh_hi[:, m], rh[:, m]).then_inc(rh_hi_ready, 1)
                        act.wait_ge(z_summed, t + 1)
                        nc.scalar.activation(z[:], pre[s][2][:, :, j], ACT.Sigmoid,
                                             scale=scale_of(BACK, Z)).then_inc(z_ready, 1)
                        if more:
                            seed(pair + 1, 1 - s, (2,) if j == 0 else (5,))
                        for m in range(NC):
                            act.wait_ge(hh_summed, NC * t + m + 1)
                            nc.scalar.activation(hh[:, m], pre_of(s, H, m)[:, j], ACT.Tanh,
                                                 scale=scale_of(BACK, H)).then_inc(hh_ready, 1)
                        seed_next = (lambda i: seed(pair + 1, 1 - s, (i + 3,))) if j == 0 else \
                                    (lambda i: seed(pair + 2, s, (i,)))
                        seeds = more if j == 0 else not (last and q >= RING - 2)
                        if seeds:
                            if j == 1:
                                act.wait_ge(hh_ready, NC * (t + 1))
                            seed_next(0)
                        for m in range(NC if more or j == 0 else 0):
                            act.wait_ge(h_ready, NC * (t + 1) + m + 1)
                            nc.scalar.copy(h_hi[:, m], h[:, j, m]).then_inc(h_hi_ready, 1)
                        if seeds:
                            seed_next(1)
                        if j == 0 and not (last and q >= RING - 2):
                            take_xt_hi(pair + 2, s)

            turns(act, body)

        @block.vector
        def _(dve):
            def take_xt_lo(pair, s, c):
                dve.wait_ge(xt_hi_ready, pair + 1)
                nc.vector.tensor_tensor(xt_lo[:, s, c], x_ps[:, c], xt_hi[:, s, c].bitcast(F32),
                                        ALU.subtract).then_inc(xt_lo_ready, 1)

            def make_y(t, par, slot, j):
                dve.wait_ge(h_turned, t + 1)
                nc.vector.scalar_tensor_tensor(out=y_ring[:, slot, j], in0=y_ps[:, par], scalar=1.0 / STATE,
                                               in1=x_ring[:, slot, j], op0=ALU.mult, op1=ALU.add).then_inc(y_ready, 1)

            def scaled(place, raw, what, g, ready):
                nc.vector.tensor_scalar(place[:, g], raw[:, g], scale_of(what, g), None, ALU.mult).then_inc(ready[g], 1)

            def make_w_lo(g):
                dve.wait_ge(w_hi_ready[g], 1)
                nc.vector.scalar_tensor_tensor(out=w_lo[:, g], in0=w_raw[:, g], scalar=scale_of(OF_SUM, g),
                                               in1=w_hi[:, g].bitcast(F32), op0=ALU.mult,
                                               op1=ALU.subtract).then_inc(w_lo_ready[g], 1)

            def make_u_lo(g):
                dve.wait_ge(u_hi_ready[g], 1)
                nc.vector.scalar_tensor_tensor(out=u_lo[:, g], in0=u[:, g], scalar=scale_of(OF_U, g),
                                               in1=u_hi[:, g], op0=ALU.mult, op1=ALU.subtract).then_inc(u_lo_ready, 1)

            nc.vector.memset(blank[:], 0.0).then_inc(blank_ready, 1)
            nc.vector.memset(ones[:], 1.0).then_inc(ones_ready, 1)
            for m in range(NC):
                nc.vector.memset(h[:, 1, m], 0.0).then_inc(h_ready, 1)
                nc.vector.memset(h_hi[:, m], 0.0).then_inc(h_hi_ready, 1)
                nc.vector.memset(h_lo[:, m], 0.0).then_inc(h_lo_ready, 1)
            for g in (R, Z, H):
                dve.wait_ge(u_loaded[g], 16)
                nc.vector.tensor_reduce(u_max[:, g:g + 1], u[:, g], mybir.AxisListType.XY, ALU.max,
                                        apply_absolute_value=True).then_inc(u_max_ready, 1)
            dve.wait_ge(u_max_turned, 1)
            nc.vector.tensor_reduce(u_max_t[:], y_ps[0:3, 0, 0:P], mybir.AxisListType.X,
                                    ALU.max).then_inc(u_max_t_ready, 1)
            dve.wait_ge(u_max_t_ready, 1)
            nc.vector.tensor_scalar(u_max_diag[:], ident[0:3, 0:3], u_max_t[:, 0:1], None,
                                    ALU.mult).then_inc(u_max_diag_ready, 1)
            dve.wait_ge(u_max_spread, 1)
            nc.vector.tensor_single_scalar(exponent[:], y_ps[:, 0, 0:3].bitcast(I32), F32_MANTISSA,
                                           ALU.logical_shift_right).then_inc(exponent_ready, 1)
            least = U_TOP + F32_BIAS - U_BITS_MAX
            of_u = U_TOP + 2 * F32_BIAS
            dve.wait_ge(exponent_ready, 1)
            nc.vector.tensor_scalar(minus_exponent[:], exponent[:], least, -1, ALU.max, ALU.mult).then_inc(field_ready, 1)
            nc.vector.tensor_scalar(fields[:, BACK], exponent[:], least, 2 * F32_BIAS - STATE_BITS - of_u, ALU.max,
                                    ALU.add).then_inc(field_ready, 1)
            dve.wait_ge(field_ready, 1)
            nc.vector.tensor_single_scalar(fields[:, OF_U], minus_exponent[:], of_u, ALU.add).then_inc(field_ready, 1)
            nc.vector.tensor_single_scalar(fields[:, OF_SUM], minus_exponent[:], of_u + STATE_BITS,
                                           ALU.add).then_inc(field_ready, 1)
            dve.wait_ge(field_ready, 4)
            nc.vector.tensor_single_scalar(scales[:], fields[:], F32_MANTISSA,
                                           ALU.logical_shift_left).then_inc(scales_ready, 1)
            dve.wait_ge(scales_ready, 1)
            dve.wait_ge(w_loaded[R], 16)
            scaled(w_hi, w_raw, OF_SUM, R, w_hi_ready)
            dve.wait_ge(bias_turned, 1)
            nc.vector.tensor_tensor(bias_scaled[:], y_ps[:, 1, 0:3 * NC].rearrange("p (g m) -> p g m", m=NC),
                                    scales[:, OF_SUM].bitcast(F32).unsqueeze(2).to_broadcast([P, 3, NC]),
                                    ALU.mult).then_inc(bias_ready, 1)
            make_w_lo(R)
            take_xt_lo(0, 0, 0)
            take_xt_lo(0, 0, 1)
            dve.wait_ge(w_loaded[H], 16)
            scaled(w_hi, w_raw, OF_SUM, H, w_hi_ready)
            make_w_lo(H)
            make_w_lo(Z)
            make_u_lo(R)
            scaled(u_hi, u, OF_U, H, u_hi_ready)
            make_u_lo(Z)
            make_u_lo(H)
            dve.wait_ge(seeded, len(TILES))
            for m in range(NC):
                nc.vector.tensor_scalar(v[:, TILES.index((Z, m))], v_sum(Z)[:, m], scale_of(OF_SUM, Z),
                                        bias_scaled[:, Z, m:m + 1], ALU.mult, ALU.add).then_inc(v_z_ready, 1)
            take_xt_lo(1, 1, 0)
            take_xt_lo(1, 1, 1)
            dve.wait_ge(x_loaded[RING - 1], 16)
            dve.wait_ge(bias_ready, 1)
            dve.sem_inc(y_ready, 1)
            dve.wait_ge(u_lo_ready, 3)

            def body(pair0, turn, last):
                for q in range(RING):
                    pair, s = pair0 + q, q % 2
                    for j in range(PAIR):
                        t, old, new = PAIR * pair + j, (j + 1) % 2, j
                        take_x = j == 1 and not (last and q >= RING - 2)
                        if take_x:
                            take_xt_lo(pair + 2, s, 0)
                        for m in range(NC):
                            dve.wait_ge(r_ready, NC * t + m + 1)
                            nc.vector.tensor_tensor(rh[:, m], r[:, m], h[:, old, m], ALU.mult).then_inc(rh_ready, 1)
                        for m in range(NC):
                            dve.wait_ge(rh_hi_ready, NC * t + m + 1)
                            nc.vector.tensor_tensor(rh_lo[:, m], rh[:, m], rh_hi[:, m], ALU.subtract).then_inc(rh_lo_ready, 1)
                        dve.wait_ge(z_ready, t + 1)
                        nc.vector.scalar_tensor_tensor(out=zh[:], in0=z[:], scalar=1.0, in1=h[:, old],
                                                       op0=ALU.subtract, op1=ALU.mult).then_inc(zh_ready, 1)
                        if take_x:
                            take_xt_lo(pair + 2, s, 1)
                        final = last and q == RING - 1 and j == 1
                        if final:
                            dve.wait_ge(y_stored[q], 16 * (turn + 1))
                            make_y(t, old, q, old)
                        for m in range(NC):
                            dve.wait_ge(hh_ready, NC * t + m + 1)
                            nc.vector.scalar_tensor_tensor(out=zhh[:, m], in0=z[:, m], scalar=STATE, in1=hh[:, m],
                                                           op0=ALU.mult, op1=ALU.mult).then_inc(zhh_ready, 1)
                        dve.wait_ge(zh_ready, t + 1)
                        for m in range(NC):
                            dve.wait_ge(zhh_ready, NC * t + m + 1)
                            nc.vector.tensor_tensor(h[:, new, m], zhh[:, m], zh[:, m],
                                                    ALU.subtract).then_inc(h_ready, 1)
                        for m in range(0 if final else NC):
                            dve.wait_ge(h_hi_ready, NC * (t + 1) + m + 1)
                            nc.vector.tensor_tensor(h_lo[:, m], h[:, new, m], h_hi[:, m],
                                                    ALU.subtract).then_inc(h_lo_ready, 1)
                        if j == 1 and not final:
                            dve.wait_ge(y_stored[q], 16 * (turn + 1))
                        if not final:
                            make_y(t, old, q if j == 1 else (q - 1) % RING, old)

            turns(dve, body)
            make_y(T, 1, RING - 1, 1)


_INS = ["x", "cond_1024"] + [f"L0_cond_{n}" for n in ("W_z", "U_z", "C_z", "b_z", "W_r", "U_r", "C_r", "b_r", "W", "U", "C", "b")]


def kernel(**inputs):
    import numpy as np
    import concourse.bacc as bacc
    from concourse.bass_utils import run_bass_kernel_spmd

    nc = bacc.Bacc("TRN2", target_bir_lowering=False, num_devices=1)
    arrays, args = {}, []
    for name in _INS:
        a = np.ascontiguousarray(inputs[name])
        arrays[f"in_{name}"] = a
        args.append(nc.dram_tensor(f"in_{name}", a.shape, mybir.dt.from_np(a.dtype), kind="ExternalInput").ap())
    out = nc.dram_tensor("out", inputs["x"].shape, F32, kind="ExternalOutput").ap()
    gated_recurrence(nc, *args, out)
    r = run_bass_kernel_spmd(nc, [arrays], core_ids=[0])
    return r.results[0]["out"]
```
